# Optimizing a Trainium2 kernel written in Bass

```python
import numpy as np
import jax
import jax.numpy as jnp

def _softmax(x, axis=-1):
    return jax.nn.softmax(x, axis=axis)

def _gelu(x):
    return jax.nn.gelu(x, approximate=True)

def _silu(x):
    return jax.nn.silu(x)

def _sigmoid(x):
    return jax.nn.sigmoid(x)

def _layernorm(x, axis=-1, eps=1e-05):
    m = jnp.mean(x, axis=axis, keepdims=True)
    v = jnp.var(x, axis=axis, keepdims=True)
    return (x - m) / jnp.sqrt(v + eps)

def _scatter_add(tgt, idx, src, axis=0):
    return tgt.at[idx].add(src)

def _segment_sum(src, seg, n):
    return jax.ops.segment_sum(src, seg, n)
kernel_name = 'mk_adaln_attn_ffn_d1_seqx_r4_0d9af4'

def setup_inputs(seed: int=0):
    np.random.seed(seed)
    _w = jnp.asarray

    def _rec_inputs():
        import jax
        import jax.numpy as jnp
        _rk = jax.random.key(seed)
        x = -0.000125 + 0.9999 * jax.random.normal(jax.random.fold_in(_rk, 1), (8, 256, 1024), jnp.float32)
        _lenS = 256 - jax.random.randint(jax.random.fold_in(_rk, 7), (8,), 0, max(1, 256 // 4) + 1, jnp.int32)
        _lenS2 = 256 - jax.random.randint(jax.random.fold_in(_rk, 8), (8,), 0, max(1, 256 // 4) + 1, jnp.int32)
        itok_B_0_23 = jax.random.randint(jax.random.fold_in(_rk, 11), (8,), 0, 24, jnp.int32)
        itok_B_6_15 = jax.random.randint(jax.random.fold_in(_rk, 12), (8,), 6, 16, jnp.int32)
        return (x, itok_B_0_23, itok_B_6_15)
    x, itok_B_0_23, itok_B_6_15 = _rec_inputs()

    def _L0_cond_setup():
        import jax, jax.numpy as jnp
        import numpy as np
        R = 16
        ALPHA = 32
        SCALING = ALPHA / R
        SLOTS = 32
        IN_F = 1024
        OUT_F = 1024
        B, T = (8, 256)
        key = jax.random.key(seed)
        k1, k2, k3, k4, k5, k6 = jax.random.split(key, 6)
        x = jax.random.normal(k1, (B, T, IN_F), dtype=jnp.float32)
        adapter_mapping = jax.random.randint(k2, (B,), 0, SLOTS, dtype=jnp.int32)
        W = jax.random.normal(k3, (OUT_F, IN_F), dtype=jnp.float32) * 0.02
        b = jax.random.normal(k4, (OUT_F,), dtype=jnp.float32) * 0.02
        lora_As = jax.random.normal(k5, (SLOTS, IN_F, R), dtype=jnp.float32) * 0.02
        lora_Bs = jax.random.normal(k6, (SLOTS, R, OUT_F), dtype=jnp.float32) * 0.02
        return {'x': x, 'adapter_mapping': adapter_mapping, 'W': W, 'b': b, 'lora_As': lora_As, 'lora_Bs': lora_Bs}
    _L0_cond_all = _L0_cond_setup()
    _L0_cond_in = {k: v for k, v in _L0_cond_all.items() if k in ('W', 'b', 'lora_As', 'lora_Bs')}
    del _L0_cond_all

    def _L0_attn_setup():
        import jax, jax.numpy as jnp
        import numpy as np
        H = 1024
        D = 2048
        N = 16
        K = 4
        R = 64
        BATCH = 1
        L = 512
        EPS = 1e-06

        def _rmsnorm(x, w):
            return x * jax.lax.rsqrt(jnp.mean(x * x, axis=-1, keepdims=True) + EPS) * w
        key = jax.random.key(seed)
        ks = jax.random.split(key, 10)
        s = 0.02
        return {'hidden_states': jax.random.normal(ks[0], (BATCH, L, H), jnp.float32), 'W_in': jax.random.normal(ks[1], (2 * D, H), jnp.float32) * s, 'conv_w': jax.random.normal(ks[2], (D, K), jnp.float32) * s, 'conv_b': jax.random.normal(ks[3], (D,), jnp.float32) * s, 'Wx': jax.random.normal(ks[4], (R + 2 * N, D), jnp.float32) * s, 'dt_ln_w': jnp.ones((R,), jnp.float32), 'b_ln_w': jnp.ones((N,), jnp.float32), 'c_ln_w': jnp.ones((N,), jnp.float32), 'Wdt': jax.random.normal(ks[5], (D, R), jnp.float32) * s, 'dt_bias': jax.random.normal(ks[6], (D,), jnp.float32) * s, 'A': -jnp.exp(jax.random.normal(ks[7], (D, N), jnp.float32) * 0.5), 'D_param': jnp.ones((D,), jnp.float32), 'W_out': jax.random.normal(ks[8], (H, D), jnp.float32) * s}
    _L0_attn_all = _L0_attn_setup()
    _L0_attn_in = {k: v for k, v in _L0_attn_all.items() if k in ('W_in', 'conv_w', 'conv_b', 'Wx', 'dt_ln_w', 'b_ln_w', 'c_ln_w', 'Wdt', 'dt_bias', 'A', 'D_param', 'W_out')}
    del _L0_attn_all

    def _L0_cond2_setup():
        import jax, jax.numpy as jnp
        import numpy as np
        B, S, D_IN, D_OUT = (4, 512, 1024, 1024)
        RANK, MAX_LORAS = (16, 32)
        key = jax.random.key(seed)
        ks = jax.random.split(key, 6)
        x = jax.random.normal(ks[0], (B, S, D_IN), dtype=jnp.float32)
        adapter_ids = jax.random.randint(ks[1], (B,), 0, MAX_LORAS)
        base_weight = jax.random.normal(ks[2], (D_OUT, D_IN), dtype=jnp.float32) * D_IN ** (-0.5)
        base_bias = jax.random.normal(ks[3], (D_OUT,), dtype=jnp.float32) * 0.01
        lora_A_w = jax.random.normal(ks[4], (MAX_LORAS, RANK, D_IN), dtype=jnp.float32) * D_IN ** (-0.5)
        lora_B_w = jax.random.normal(ks[5], (MAX_LORAS, D_OUT, RANK), dtype=jnp.float32) * RANK ** (-0.5)
        return {'x': x, 'adapter_ids': adapter_ids, 'base_weight': base_weight, 'base_bias': base_bias, 'lora_A_w': lora_A_w, 'lora_B_w': lora_B_w}
    _L0_cond2_all = _L0_cond2_setup()
    _L0_cond2_in = {k: v for k, v in _L0_cond2_all.items() if k in ('base_weight', 'base_bias', 'lora_A_w', 'lora_B_w')}
    del _L0_cond2_all

    def _L0_ffn_setup():
        import jax, jax.numpy as jnp
        import numpy as np
        N_EXPERTS = 8
        TOP_K = 2
        D_MODEL = 1024
        RANK = 64
        key = jax.random.key(seed)
        k0, k1, k2, k3 = jax.random.split(key, 4)
        inputs = jax.random.normal(k0, (4, 512, D_MODEL), dtype=jnp.float32)
        gate_w = jax.random.normal(k1, (N_EXPERTS, D_MODEL), dtype=jnp.float32) * 0.02
        lora_A = jax.random.normal(k2, (N_EXPERTS, RANK, D_MODEL), dtype=jnp.float32) * 0.02
        lora_B = jax.random.normal(k3, (N_EXPERTS, D_MODEL, RANK), dtype=jnp.float32) * 0.02
        return {'inputs': inputs, 'gate_w': gate_w, 'lora_A': lora_A, 'lora_B': lora_B}
    _L0_ffn_all = _L0_ffn_setup()
    _L0_ffn_in = {k: v for k, v in _L0_ffn_all.items() if k in ('gate_w', 'lora_A', 'lora_B')}
    del _L0_ffn_all
    return {'x': x, 'itok_B_0_23': itok_B_0_23, 'itok_B_6_15': itok_B_6_15, 'L0_cond_W': _L0_cond_in['W'], 'L0_cond_b': _L0_cond_in['b'], 'L0_cond_lora_As': _L0_cond_in['lora_As'], 'L0_cond_lora_Bs': _L0_cond_in['lora_Bs'], 'L0_attn_W_in': _L0_attn_in['W_in'], 'L0_attn_conv_w': _L0_attn_in['conv_w'], 'L0_attn_conv_b': _L0_attn_in['conv_b'], 'L0_attn_Wx': _L0_attn_in['Wx'], 'L0_attn_dt_ln_w': _L0_attn_in['dt_ln_w'], 'L0_attn_b_ln_w': _L0_attn_in['b_ln_w'], 'L0_attn_c_ln_w': _L0_attn_in['c_ln_w'], 'L0_attn_Wdt': _L0_attn_in['Wdt'], 'L0_attn_dt_bias': _L0_attn_in['dt_bias'], 'L0_attn_A': _L0_attn_in['A'], 'L0_attn_D_param': _L0_attn_in['D_param'], 'L0_attn_W_out': _L0_attn_in['W_out'], 'L0_cond2_base_weight': _L0_cond2_in['base_weight'], 'L0_cond2_base_bias': _L0_cond2_in['base_bias'], 'L0_cond2_lora_A_w': _L0_cond2_in['lora_A_w'], 'L0_cond2_lora_B_w': _L0_cond2_in['lora_B_w'], 'L0_ffn_gate_w': _L0_ffn_in['gate_w'], 'L0_ffn_lora_A': _L0_ffn_in['lora_A'], 'L0_ffn_lora_B': _L0_ffn_in['lora_B']}

def reference(x, itok_B_0_23, itok_B_6_15, L0_cond_W, L0_cond_b, L0_cond_lora_As, L0_cond_lora_Bs, L0_attn_W_in, L0_attn_conv_w, L0_attn_conv_b, L0_attn_Wx, L0_attn_dt_ln_w, L0_attn_b_ln_w, L0_attn_c_ln_w, L0_attn_Wdt, L0_attn_dt_bias, L0_attn_A, L0_attn_D_param, L0_attn_W_out, L0_cond2_base_weight, L0_cond2_base_bias, L0_cond2_lora_A_w, L0_cond2_lora_B_w, L0_ffn_gate_w, L0_ffn_lora_A, L0_ffn_lora_B):
    import jax
    import jax.numpy as jnp

    def _L0_cond_ref(x, adapter_mapping, W, b, lora_As, lora_Bs):
        import jax, jax.numpy as jnp
        import numpy as np
        R = 16
        ALPHA = 32
        SCALING = ALPHA / R
        SLOTS = 32
        IN_F = 1024
        OUT_F = 1024
        B, T = (8, 256)
        base_out = jnp.einsum('bti,oi->bto', x, W) + b
        A = lora_As[adapter_mapping]
        Bm = lora_Bs[adapter_mapping]
        lora_h = jnp.einsum('bti,bir->btr', x, A)
        lora_out = jnp.einsum('btr,bro->bto', lora_h, Bm)
        return base_out + lora_out * SCALING

    def _L0_attn_ref(hidden_states, W_in, conv_w, conv_b, Wx, dt_ln_w, b_ln_w, c_ln_w, Wdt, dt_bias, A, D_param, W_out):
        import jax, jax.numpy as jnp
        import numpy as np
        H = 1024
        D = 2048
        N = 16
        K = 4
        R = 64
        BATCH = 1
        L = 512
        EPS = 1e-06

        def _rmsnorm(x, w):
            return x * jax.lax.rsqrt(jnp.mean(x * x, axis=-1, keepdims=True) + EPS) * w
        proj = hidden_states @ W_in.T
        u, gate = jnp.split(proj, 2, axis=-1)
        x = jnp.transpose(u, (0, 2, 1))
        x = jax.lax.conv_general_dilated(x, conv_w[:, None, :], window_strides=(1,), padding=[(K - 1, 0)], dimension_numbers=('NCH', 'OIH', 'NCH'), feature_group_count=D)
        u = jax.nn.silu(jnp.transpose(x, (0, 2, 1)) + conv_b)
        ssm_p = u @ Wx.T
        dt, Bm, Cm = jnp.split(ssm_p, [R, R + N], axis=-1)
        dt = _rmsnorm(dt, dt_ln_w)
        Bm = _rmsnorm(Bm, b_ln_w)
        Cm = _rmsnorm(Cm, c_ln_w)
        delta = jax.nn.softplus(dt @ Wdt.T + dt_bias)

        def step(state, xs):
            d_t, B_t, C_t, u_t = xs
            dA = jnp.exp(d_t[..., None] * A)
            state = dA * state + (d_t * u_t)[..., None] * B_t[:, None, :]
            y_t = jnp.einsum('bdn,bn->bd', state, C_t)
            return (state, y_t)
        init = jnp.zeros((hidden_states.shape[0], D, N), hidden_states.dtype)
        xs = (jnp.swapaxes(delta, 0, 1), jnp.swapaxes(Bm, 0, 1), jnp.swapaxes(Cm, 0, 1), jnp.swapaxes(u, 0, 1))
        _, ys = jax.lax.scan(step, init, xs)
        y = jnp.swapaxes(ys, 0, 1) + u * D_param
        y = y * jax.nn.silu(gate)
        return y @ W_out.T

    def _L0_cond2_ref(x, adapter_ids, base_weight, base_bias, lora_A_w, lora_B_w):
        import jax, jax.numpy as jnp
        import numpy as np
        B, S, D_IN, D_OUT = (4, 512, 1024, 1024)
        RANK, MAX_LORAS = (16, 32)
        result = jnp.einsum('bsd,od->bso', x, base_weight) + base_bias
        A = lora_A_w[adapter_ids]
        Bw = lora_B_w[adapter_ids]
        h = jnp.einsum('bsd,brd->bsr', x, A)
        lora_out = jnp.einsum('bsr,bor->bso', h, Bw)
        result = result + lora_out
        return result.astype(x.dtype)

    def _L0_ffn_ref(inputs, gate_w, lora_A, lora_B):
        import jax, jax.numpy as jnp
        import numpy as np
        N_EXPERTS = 8
        TOP_K = 2
        D_MODEL = 1024
        RANK = 64
        x = inputs.reshape(-1, inputs.shape[-1])
        T = x.shape[0]
        gate_probs = jax.nn.softmax(x @ gate_w.T, axis=-1)
        weights, sel = jax.lax.top_k(gate_probs, TOP_K)
        weights = weights / jnp.sum(weights, axis=-1, keepdims=True)
        w_full = jnp.zeros((T, N_EXPERTS), dtype=x.dtype).at[jnp.arange(T)[:, None], sel].add(weights)
        out = jnp.zeros((T, D_MODEL), dtype=x.dtype)
        for e in range(N_EXPERTS):
            y = x @ lora_A[e].T @ lora_B[e].T
            out = out + w_full[:, e:e + 1] * y
        return out.reshape(inputs.shape[:-1] + (D_MODEL,))
    x = x + _L0_attn_ref(_L0_cond_ref(x, itok_B_0_23, L0_cond_W, L0_cond_b, L0_cond_lora_As, L0_cond_lora_Bs), L0_attn_W_in, L0_attn_conv_w, L0_attn_conv_b, L0_attn_Wx, L0_attn_dt_ln_w, L0_attn_b_ln_w, L0_attn_c_ln_w, L0_attn_Wdt, L0_attn_dt_bias, L0_attn_A, L0_attn_D_param, L0_attn_W_out)
    x = x + _L0_ffn_ref(_L0_cond2_ref(x, itok_B_6_15, L0_cond2_base_weight, L0_cond2_base_bias, L0_cond2_lora_A_w, L0_cond2_lora_B_w), L0_ffn_gate_w, L0_ffn_lora_A, L0_ffn_lora_B)
    return x

_drawn_inputs = setup_inputs


def setup_inputs(seed=0):
    import zlib

    import numpy as np

    out = dict(_drawn_inputs(seed))
    spreads = {'L0_attn_dt_ln_w': (1.0, 0.6),
     'L0_attn_b_ln_w': (1.0, 0.6),
     'L0_attn_c_ln_w': (1.0, 0.6),
     'L0_attn_D_param': (1.0, 0.6)}
    factors = {'L0_cond_W': 3.56,
     'L0_cond_b': 8.0,
     'L0_cond_lora_As': 8.0,
     'L0_cond_lora_Bs': 8.0,
     'L0_attn_W_in': 3.557,
     'L0_attn_conv_w': 4.728,
     'L0_attn_conv_b': 4.315,
     'L0_attn_Wx': 3.929,
     'L0_attn_Wdt': 8.0,
     'L0_attn_dt_bias': 8.0,
     'L0_attn_A': 8.0,
     'L0_attn_W_out': 3.578,
     'L0_cond2_base_bias': 8.0}
    for name, (base, spread) in spreads.items():
        noise = np.random.default_rng([zlib.crc32(name.encode()), seed]).standard_normal(out[name].shape)
        drawn = base * np.exp(spread * noise) if base else spread * noise
        out[name] = jnp.asarray(drawn.astype(out[name].dtype))
    for name, factor in factors.items():
        out[name] = (out[name] * factor).astype(out[name].dtype)
    return out
```

```python
from contextlib import ExitStack

import numpy as np
import concourse.bass as bass
import concourse.mybir as mybir
from concourse.alu_op_type import AluOpType as ALU

F32 = mybir.dt.float32
I32 = mybir.dt.int32
U32 = mybir.dt.uint32
ACT = mybir.ActivationFunctionType
AX = mybir.AxisListType

P = 128
B = 8
T = 256
H = 1024
KH = H // P
D = 2048
NC = D // P
N = 16
R = 64
RX = R + 2 * N
TAPS = 4
LR = 16
SLOTS = 32
E = 8
ER = 64
EK = E * ER // P
Q = 4
NQ = N // Q
QT = NQ * T
PAIRS = NC // 2
LAST = B - 1

OUT_TILES = 2 * KH
G_TILES = EK
COND_TILES = KH
LB_TILES = KH // 2
RING = 4
PRO_TILES = KH + 2 * COND_TILES


def has_cond(g):
    return not isinstance(g, int) or g + 2 < B


def has_next(g):
    return not isinstance(g, int) or g + 1 < B


def tiles_before(g):
    n = PRO_TILES + (OUT_TILES + G_TILES + COND_TILES + LB_TILES) * g
    return n - COND_TILES if isinstance(g, int) and g == B - 1 else n


def tile_round(g, idx):
    n = PRO_TILES // RING + (OUT_TILES + G_TILES + COND_TILES + LB_TILES) // RING * g
    if isinstance(g, int) and g == B - 1:
        n -= COND_TILES // RING
    return n + idx // RING


def build(nc, x, idx_cond, idx_cond2, cond_W, cond_b, cond_A, cond_B, W_in, conv_w, conv_b, Wx, ln_w, Wdt, dt_bias,
          A_mat, D_par, W_out, base_W, base_b, lora2_A, lora2_B, GT_gate, GT_exp, ffn_B,
          ident_in, mean_in, sel_in, iota_in, out):
    with ExitStack() as ctx:
        def sb(name, shape, dt=F32):
            return ctx.enter_context(nc.sbuf_tensor(name, shape, dt))

        def sem(name):
            return ctx.enter_context(nc.semaphore(name))

        bc_rows = nc.dram_tensor("bc_rows", (B, 2 * N, T), F32, kind="Internal").ap()
        G_tiles = nc.dram_tensor("G_tiles", (EK, P, KH, P), F32, kind="Internal").ap()
        b2g_rows = nc.dram_tensor("b2g_rows", (B, LR, E * ER + E), F32, kind="Internal").ap()

        ident = sb("ident", [P, P])
        mean_w = sb("mean_w", [RX, RX])
        sel = sb("sel", [E, E * ER])
        iota = sb("iota", [P, E])
        ones_row = sb("ones_row", [1, P])
        idx_sb = sb("idx_sb", [1, 2 * B], I32)
        wdt = sb("wdt", [R, D])
        dtb = sb("dtb", [P, NC])
        A_sb = sb("A_sb", [P, NC * N])
        D_sb = sb("D_sb", [P, NC])
        cw = sb("cw", [P, NC, TAPS])
        cb = sb("cb", [P, NC])
        lnw = sb("lnw", [RX, 1])
        cond_bias = sb("cond_bias", [P, KH])
        base_bias = sb("base_bias", [P, KH])
        g_gate = sb("g_gate", [P, KH, E])
        g_bias = sb("g_bias", [P, EK])
        gate_bias = sb("gate_bias", [1, E])
        eps = sb("eps", [RX, 1])

        gate_w = sb("gate_w", [P, 2, KH, P])
        u_w = sb("u_w", [P, 2, KH, P])
        wx_w = sb("wx_w", [P, 2, RX])
        m_w = sb("m_w", [P, RING, KH, P])
        cA = sb("cA", [P, KH, LR])
        cB = sb("cB", [LR, H])
        c2A = sb("c2A", [P, KH, LR])
        b2g = sb("b2g", [LR, E * ER + E])

        xb = sb("xb", [P, KH, T])
        h0 = sb("h0", [P, 2, KH, T])
        u_sb = sb("u_sb", [P, NC, T])
        dy = sb("dy", [P, NC, T])
        bc = sb("bc", [P, 2, N, T])
        dA = sb("dA", [P, Q, NQ, T])
        st = sb("st", [P, Q, NQ, T])
        w_sb = sb("w_sb", [P, 2, T])
        up = sb("up", [P, 2, T + TAPS - 1])
        cv = sb("cv", [P, 2, T])
        th = sb("th", [P, 2, T])
        gh = sb("gh", [P, 2, T])
        gt = sb("gt", [P, 2, T])
        y1 = sb("y1", [P, T])
        xs = sb("xs", [RX, T])
        sq = sb("sq", [RX, T])
        rr = sb("rr", [RX, T])
        nrm = sb("nrm", [RX, T])
        la = sb("la", [LR, T])
        la2 = sb("la2", [LR, T])
        x2 = sb("x2", [P, KH, T])
        hw = sb("hw", [P, EK, T])
        lg = sb("lg", [P, 2, E])
        lm = sb("lm", [P, 2, E])
        ex = sb("ex", [P, 2, E])
        pr = sb("pr", [P, 2, E])
        pr_copy = sb("pr_copy", [P, 2, E])
        top = sb("top", [P, 2, E])
        tix = sb("tix", [P, 2, E], U32)
        tixf = sb("tixf", [P, 2, E])
        oh = sb("oh", [P, 2, 2, E])
        wf = sb("wf", [P, 2, E])
        sc = sb("sc", [P, 5, 2])
        w01 = sb("w01", [P, 2, 2])
        wT = sb("wT", [E, T])

        gt_all = bc[:, :, :, :].rearrange("p a n t -> p (a n t)")
        GTx = gt_all[:, 0:KH * E * ER].rearrange("p (k g) -> p k g", k=KH)
        GTg = gt_all[:, KH * E * ER:KH * (E * ER + E)].rearrange("p (k g) -> p k g", k=KH)
        b2_all = u_sb[:, 0:4, :].rearrange("p c t -> p (c t)").rearrange("p (k b r) -> p k b r", b=B, k=KH)
        stage = [st[:, i, :, :].rearrange("p n t -> p (n t)")[:, 0:E * ER] for i in range(2)]
        b2g_stage = st[:, 2, :, :].rearrange("p n t -> p (n t)")[:, 0:E * ER + E]

        bank = [ctx.enter_context(nc.psum_tensor(f"bank{i}", [P, 512], F32)) for i in range(8)]
        Dring = [bank[0], bank[1]]
        ps_gate, ps_u, ps_x = bank[2], bank[3], bank[4]
        Yring = [bank[5], bank[6]]
        S = bank[7]

        consts_ld = sem("consts_ld")
        idx_ld = sem("idx_ld")
        gt_ld = sem("gt_ld")
        b2_ld = sem("b2_ld")
        gate_ld = [sem("gate_ld0"), sem("gate_ld1")]
        u_ld = [sem("u_ld0"), sem("u_ld1")]
        wx_ld = [sem("wx_ld0"), sem("wx_ld1")]
        m_ld = [sem(f"m_ld{i}") for i in range(RING)]
        cond_ld = sem("cond_ld")
        ffn_ld = sem("ffn_ld")
        bc_st = sem("bc_st")
        bc_ld = sem("bc_ld")
        G_st = [sem("G_st0"), sem("G_st1")]
        b2g_st = sem("b2g_st")
        out_st = sem("out_st")
        set_up = sem("set_up")
        halved = sem("halved")
        gate_mm = sem("gate_mm")
        gate_ev = sem("gate_ev")
        u_mm = sem("u_mm")
        u_ev = sem("u_ev")
        wx_mm = sem("wx_mm")
        x_ev = sem("x_ev")
        ms_mm = sem("ms_mm")
        ms_ev = sem("ms_ev")
        act_step = sem("act_step")
        r_done = sem("r_done")
        nrm_done = sem("nrm_done")
        z_mm = sem("z_mm")
        z_ev = sem("z_ev")
        sp_step = sem("sp_step")
        delta_done = sem("delta_done")
        conv_step = sem("conv_step")
        th_done = sem("th_done")
        u_done = sem("u_done")
        dA_done = sem("dA_done")
        w_done = sem("w_done")
        dbu_done = sem("dbu_done")
        scan_done = sem("scan_done")
        hc_done = sem("hc_done")
        y_mm = sem("y_mm")
        y_step = sem("y_step")
        y_done = sem("y_done")
        m_mm = sem("m_mm")
        d_ev = sem("d_ev")
        h_ev = sem("h_ev")
        c_ev = sem("c_ev")
        la_mm = sem("la_mm")
        la_ev = sem("la_ev")
        la2_mm = sem("la2_mm")
        la2_ev = sem("la2_ev")
        lg_mm = sem("lg_mm")
        lg_ev = sem("lg_ev")
        soft = sem("soft")
        ex_done = sem("ex_done")
        wf_done = sem("wf_done")
        wT_mm = sem("wT_mm")
        wT_ev = sem("wT_ev")
        wb_mm = sem("wb_mm")
        G_mm = sem("G_mm")
        G_ev = sem("G_ev")
        gs_mm = sem("gs_mm")
        gs_ev = sem("gs_ev")

        block = ctx.enter_context(nc.Block())
        N_CONSTS = 15
        PRO_D = KH
        D_USES = KH + EK + KH
        SOFT_STEPS = 16

        @block.sync
        def _(sp):
            def load_tile(n_round, slot, used, src):
                sp.wait_ge(m_mm, used)
                sp.dma_start(m_w[:, slot], src).then_inc(m_ld[slot], 16)

            def load_cond(j):
                rA = sp.value_load(idx_sb[0:1, bass.ds(j, 1)], min_val=0, max_val=SLOTS - 1)
                sp.dma_start(xb[:, :, :], x[bass.ds(j, 1)].rearrange("a p k t -> p (a k) t")).then_inc(cond_ld, 16)
                sp.dma_start(cA[:, :, :], cond_A[bass.ds(rA, 1)].rearrange("a p k r -> p (a k) r")).then_inc(cond_ld, 16)
                sp.dma_start(cB[:, :], cond_B[bass.ds(rA, 1)].rearrange("a r o -> r (a o)")).then_inc(cond_ld, 16)

            def u_tile(v, m, slot):
                sp.wait_ge(u_mm, v + 1)
                sp.dma_start(u_w[:, slot], W_in[bass.ds(m, 1)].rearrange("a p k o -> p (a k) o")).then_inc(u_ld[slot], 16)
                sp.wait_ge(wx_mm, v + 1)
                sp.dma_start(wx_w[:, bass.ds(slot, 1), :],
                             Wx[bass.ds(m, 1)].rearrange("a p r -> p a r")).then_inc(wx_ld[slot], 16)

            for dst, src in ((ident, ident_in), (mean_w, mean_in), (sel, sel_in), (iota, iota_in), (wdt, Wdt),
                             (dtb, dt_bias), (A_sb, A_mat), (D_sb, D_par), (cb, conv_b), (cond_bias, cond_b),
                             (base_bias, base_b)):
                sp.dma_start(dst[:, :], src).then_inc(consts_ld, 16)
            sp.dma_start(cw[:, :, :], conv_w).then_inc(consts_ld, 16)
            for i, part in enumerate(ln_w):
                lo = (0, R, R + N)[i]
                sp.dma_start(lnw[lo:lo + part.shape[0], :], part).then_inc(consts_ld, 16)
            sp.dma_start(idx_sb[:, 0:B], idx_cond).then_inc(idx_ld, 16)
            sp.dma_start(idx_sb[:, B:2 * B], idx_cond2).then_inc(idx_ld, 16)
            sp.dma_start(GTx, GT_exp).then_inc(gt_ld, 16)
            sp.dma_start(GTg, GT_gate).then_inc(gt_ld, 16)
            sp.wait_ge(idx_ld, 32)
            with sp.Fori(0, B) as b:
                r2 = sp.value_load(idx_sb[0:1, bass.ds(b + B, 1)], min_val=0, max_val=SLOTS - 1)
                sp.dma_start(b2_all[:, :, bass.ds(b, 1), :],
                             lora2_B[bass.ds(r2, 1)].rearrange("a p k r -> p k a r")).then_inc(b2_ld, 16)
            for m in range(KH):
                load_tile(m // RING, m % RING, m + 1, base_W[m])
            load_cond(0)
            for m in range(KH):
                load_tile(0, m % RING, KH + m + 1, cond_W[m])
            sp.wait_ge(m_mm, RING + 2 * KH)
            load_cond(1)
            for m in range(KH):
                load_tile(0, m % RING, 2 * KH + m + 1, cond_W[m])
            with sp.Fori(0, PAIRS) as p:
                for e in range(2):
                    u_tile(2 * p + e, 2 * p + e, e)

            def group(g):
                with sp.Fori(0, PAIRS) as p:
                    for e in range(2):
                        s = NC * g + 2 * p + e
                        sp.wait_ge(gate_mm, s + 1)
                        sp.dma_start(gate_w[:, e], W_in[bass.ds(2 * p + (NC + e), 1)].rearrange("a p k o -> p (a k) o")
                                     ).then_inc(gate_ld[e], 16)
                        if has_next(g):
                            u_tile(s + NC, 2 * p + e, e)
                tb = tiles_before(g)
                sp.wait_ge(m_mm, RING + tb)
                if has_cond(g):
                    load_cond(g + 2)
                sp.wait_ge(out_st, 32 * g + 16)
                r2 = sp.value_load(idx_sb[0:1, bass.ds(g + B, 1)], min_val=0, max_val=SLOTS - 1)
                sp.dma_start(x2[:, :, :], x[bass.ds(g, 1)].rearrange("a p k t -> p (a k) t")).then_inc(ffn_ld, 16)
                sp.dma_start(c2A[:, :, :], lora2_A[bass.ds(r2, 1)].rearrange("a p k r -> p (a k) r")).then_inc(ffn_ld, 16)
                sp.dma_start(b2g[:, :], b2g_rows[bass.ds(g, 1)].rearrange("a r o -> r (a o)")).then_inc(ffn_ld, 16)
                srcs = [W_out[m, h] for m in range(KH) for h in range(2)] + [G_tiles[m] for m in range(EK)]
                if has_cond(g):
                    srcs += [cond_W[m] for m in range(KH)]
                srcs += [ffn_B[j] for j in range(LB_TILES)]
                for i, src in enumerate(srcs):
                    load_tile(0, i % RING, tb + i + 1, src)

            for i in range(2):
                sp.wait_ge(G_st[i], 16 * KH // 2)
            sp.wait_ge(b2g_st, 16)
            with sp.Fori(0, B - 2) as g:
                group(g)
            group(B - 2)
            group(B - 1)

        @block.tensor
        def _(pe):
            mm = nc.tensor.matmul

            def cond(j, tb, rnd):
                pe.wait_ge(cond_ld, 48 * j + 48)
                for k in range(KH):
                    last = mm(S[0:LR, 0:T], cA[:, k, :], xb[:, k, :], start=(k == 0), stop=(k == KH - 1))
                last.then_inc(la_mm, 1)
                pe.wait_ge(la_ev, j + 1)
                for m in range(KH):
                    if m >= 2:
                        pe.wait_ge(c_ev, KH * j + m - 1)
                    pe.wait_ge(m_ld[m % RING], 16 * (rnd + m // RING + 1))
                    mm(Yring[m % 2][:, 0:T], cB[:, m * P:(m + 1) * P], la[:, :], start=True, stop=False)
                    for k in range(KH):
                        last = mm(Yring[m % 2][:, 0:T], m_w[:, m % RING, k, :], xb[:, k, :],
                                  start=False, stop=(k == KH - 1))
                    last.then_inc(m_mm, 1)

            def u_chunk(v, par, e, rnd):
                pe.wait_ge(u_ev, v)
                pe.wait_ge(u_ld[e], 16 * rnd + 16)
                for k in range(KH):
                    last = mm(ps_u[:, 0:T], u_w[:, e, k, :], h0[:, par, k, :],
                              start=(k == 0), stop=(k == KH - 1))
                last.then_inc(u_mm, 1)

            def x_chunk(v, c, e, rnd, start, stop):
                pe.wait_ge(u_done, v + 3)
                pe.wait_ge(wx_ld[e], 16 * rnd + 16)
                mm(ps_x[0:RX, 0:T], wx_w[:, e, :], u_sb[:, bass.ds(c, 1), :].rearrange("p a t -> p (a t)"),
                   start=start, stop=stop).then_inc(wx_mm, 1)

            def mean_square(j):
                pe.wait_ge(act_step, 2 * j + 2)
                mm(S[0:RX, 0:T], mean_w[:, :], sq[:, :], start=True, stop=True).then_inc(ms_mm, 1)

            def dt_proj(j):
                pe.wait_ge(nrm_done, j + 1)
                for c in range(NC):
                    if c >= 2:
                        pe.wait_ge(z_ev, NC * j + c - 1)
                    mm(Yring[c % 2][:, 0:T], wdt[:, c * P:(c + 1) * P], nrm[0:R, :],
                       start=True, stop=True).then_inc(z_mm, 1)

            pe.wait_ge(gt_ld, 32)
            pe.wait_ge(consts_ld, 16 * N_CONSTS)
            for m in range(KH):
                pe.wait_ge(m_ld[m % RING], 16 * (m // RING + 1))
                if m >= 2:
                    pe.wait_ge(G_ev, m - 1)
                for k in range(KH):
                    last = mm(Dring[m % 2][:, :], m_w[:, m % RING, k, :], GTx[:, k, :],
                              start=(k == 0), stop=(k == KH - 1))
                last.then_inc(G_mm, 1)
                for k in range(KH):
                    last = mm(S[:, m * E:(m + 1) * E], m_w[:, m % RING, k, :], GTg[:, k, :],
                              start=(k == 0), stop=(k == KH - 1))
                last.then_inc(m_mm, 1)
            for j in range(EK):
                for k in range(KH):
                    mm(S[:, 64 + j:65 + j], GTx[:, k, j * P:(j + 1) * P], base_bias[:, k:k + 1],
                       start=(k == 0), stop=(k == KH - 1))
            for k in range(KH):
                mm(S[0:1, 72:72 + E], base_bias[:, k:k + 1], GTg[:, k, :], start=(k == 0), stop=(k == KH - 1))
            pe.wait_ge(b2_ld, 16 * B)
            for k in range(KH):
                mm(S[:, 80:80 + E], b2_all[:, k, :, :].rearrange("p b r -> p (b r)"), GTg[:, k, :], start=(k == 0), stop=(k == KH - 1))
            for k in range(KH):
                last = mm(Yring[0][:, :], b2_all[:, k, :, :].rearrange("p b r -> p (b r)"), GTx[:, k, :], start=(k == 0), stop=(k == KH - 1))
            last.then_inc(gs_mm, 1)
            pe.wait_ge(gs_ev, 1)
            cond(0, KH, KH // RING)
            pe.wait_ge(c_ev, KH)
            cond(1, 2 * KH, 2 * KH // RING)
            u_chunk(0, 0, 0, 0)
            u_chunk(1, 0, 1, 0)
            x_chunk(0, 0, 0, 0, True, False)
            with pe.Fori(1, PAIRS) as p:
                u_chunk(2 * p, 0, 0, p)
                x_chunk(2 * p - 1, 2 * p - 1, 1, p - 1, False, False)
                u_chunk(2 * p + 1, 0, 1, p)
                x_chunk(2 * p, 2 * p, 0, p, False, False)
            x_chunk(NC - 1, NC - 1, 1, PAIRS - 1, False, True)
            mean_square(0)
            pe.wait_ge(c_ev, 2 * KH)
            dt_proj(0)

            def slots(g, p, first):
                for e in range(2):
                    c = 2 * p + e
                    s = NC * g + c
                    v = s + NC
                    pe.wait_ge(gate_ev, s + 1)
                    pe.wait_ge(gate_ld[e], 16 * (PAIRS * g + p) + 16)
                    for k in range(KH):
                        last = mm(ps_gate[:, 0:T], gate_w[:, e, k, :],
                                  h0[:, bass.ds(g % 2, 1), k, :].rearrange("p a t -> p (a t)"),
                                  start=(k == 0), stop=(k == KH - 1))
                    last.then_inc(gate_mm, 1)
                    if has_next(g):
                        pe.wait_ge(u_ev, v)
                        pe.wait_ge(u_ld[e], 16 * (PAIRS * (g + 1) + p) + 16)
                        for k in range(KH):
                            last = mm(ps_u[:, 0:T], u_w[:, e, k, :],
                                      h0[:, bass.ds((g + 1) % 2, 1), k, :].rearrange("p a t -> p (a t)"),
                                      start=(k == 0), stop=(k == KH - 1))
                        last.then_inc(u_mm, 1)
                    pe.wait_ge(y_done, s + 1)
                    for q in range(Q):
                        pe.wait_ge(hc_done, Q * s + q + 1)
                        for n in range(NQ):
                            last = mm(Yring[e][:, 0:T], ident[:, :], st[:, q, n, :],
                                      start=(q == 0 and n == 0), stop=(q == Q - 1 and n == NQ - 1))
                        last.then_inc(y_mm, 1)
                        if q == 3 and has_next(g) and not (first and e == 0):
                            if first:
                                pe.wait_ge(x_ev, g + 1)
                            x_chunk(v - 1, c - 1, 1 - e, PAIRS * (g + 1) + (p if e else p - 1),
                                    first, False)

            def group(g):
                tb = tiles_before(g)
                pe.wait_ge(z_ev, NC * (g + 1))
                if has_cond(g):
                    pe.wait_ge(c_ev, KH * (g + 2))
                pe.wait_ge(h_ev, EK * g + 1)
                slots(g, 0, True)
                with pe.Fori(1, PAIRS) as p:
                    slots(g, p, False)
                if has_next(g):
                    x_chunk(NC * (g + 2) - 1, NC - 1, 1, PAIRS * (g + 2) - 1, False, True)

                pe.wait_ge(y_done, NC * (g + 1) + 2)
                for m in range(KH):
                    i = m
                    pe.wait_ge(d_ev, PRO_D + D_USES * g + i + 1)
                    for h in range(2):
                        t = 2 * m + h
                        pe.wait_ge(m_ld[t % RING], 16 * (tile_round(g, t) + 1))
                        for k in range(KH):
                            last = mm(Dring[i % 2][:, 0:T], m_w[:, t % RING, k, :], dy[:, h * KH + k, :],
                                      start=(h == 0 and k == 0), stop=(h == 1 and k == KH - 1))
                        last.then_inc(m_mm, 1)
                    if m == 3 and has_next(g):
                        pe.wait_ge(wT_ev, g + 1)
                        mean_square(g + 1)
                if has_next(g):
                    dt_proj(g + 1)

                pe.wait_ge(ffn_ld, 48 * g + 48)
                pe.wait_ge(d_ev, PRO_D + D_USES * g + KH + 2)
                if has_next(g):
                    pe.wait_ge(ms_ev, g + 2)
                for k in range(KH):
                    last = mm(S[0:LR, 0:T], c2A[:, k, :], x2[:, k, :], start=(k == 0), stop=(k == KH - 1))
                last.then_inc(la2_mm, 1)
                pe.wait_ge(la2_ev, g + 1)
                for tc in range(2):
                    tok = slice(tc * P, (tc + 1) * P)
                    o = S[:, tc * E:(tc + 1) * E]
                    for k in range(KH):
                        mm(o, x2[:, k, tok], g_gate[:, k, :], start=(k == 0), stop=False)
                    mm(o, la2[:, tok], b2g[:, E * ER:E * ER + E], start=False, stop=False)
                    last = mm(o, ones_row[:, :], gate_bias[:, :], start=False, stop=True)
                last.then_inc(lg_mm, 1)
                for m in range(EK):
                    t = OUT_TILES + m
                    if m >= 2:
                        pe.wait_ge(h_ev, EK * g + m)
                    elif has_next(g):
                        pe.wait_ge(z_ev, NC * (g + 2))
                    pe.wait_ge(m_ld[t % RING], 16 * (tile_round(g, t) + 1))
                    mm(Yring[m % 2][:, 0:T], b2g[:, m * P:(m + 1) * P], la2[:, :], start=True, stop=False)
                    for k in range(KH):
                        last = mm(Yring[m % 2][:, 0:T], m_w[:, t % RING, k, :], x2[:, k, :],
                                  start=False, stop=(k == KH - 1))
                    last.then_inc(m_mm, 1)
                if has_cond(g):
                    pe.wait_ge(lg_ev, g + 1)
                    pe.wait_ge(h_ev, EK * g + EK + 1)
                    cond(g + 2, tb + OUT_TILES + G_TILES, tile_round(g, OUT_TILES + G_TILES))
                pe.wait_ge(wf_done, g + 1)
                for tc in range(2):
                    last = nc.tensor.transpose(S[0:E, tc * P:(tc + 1) * P], wf[:, tc, :], ident[:, :])
                last.then_inc(wT_mm, 1)
                pe.wait_ge(wT_ev, g + 2)
                for m in range(EK):
                    i = KH + m
                    pe.wait_ge(d_ev, PRO_D + D_USES * g + i + 1)
                    mm(Dring[i % 2][:, 0:T], sel[:, m * P:(m + 1) * P], wT[:, :],
                       start=True, stop=True).then_inc(wb_mm, 1)
                pe.wait_ge(d_ev, PRO_D + D_USES * g + KH + EK + 2)
                for m in range(KH):
                    i = KH + EK + m
                    t = OUT_TILES + G_TILES + (COND_TILES if has_cond(g) else 0) + m // 2
                    pe.wait_ge(d_ev, PRO_D + D_USES * g + i + 1)
                    pe.wait_ge(m_ld[t % RING], 16 * (tile_round(g, t) + 1))
                    for k in range(EK):
                        last = mm(Dring[i % 2][:, 0:T], m_w[:, t % RING, (m % 2) * EK + k, :], hw[:, k, :],
                                  start=(k == 0), stop=(k == EK - 1))
                    if m % 2:
                        last.then_inc(m_mm, 1)

            with pe.Fori(0, B - 2) as g:
                group(g)
            group(B - 2)
            group(B - 1)

        @block.scalar
        def _(act):
            fn = nc.scalar.activation

            def cond(j, par, tb):
                act.wait_ge(la_mm, j + 1)
                fn(la[:, :], S[0:LR, 0:T], ACT.Copy, scale=2.0).then_inc(la_ev, 1)
                for m in range(KH):
                    act.wait_ge(m_mm, RING + tb + m + 1)
                    fn(h0[:, par, m, :] if isinstance(par, int) else
                       h0[:, bass.ds(par, 1), m, :].rearrange("p a t -> p (a t)"),
                       Yring[m % 2][:, 0:T], ACT.Identity, bias=cond_bias[:, m:m + 1]).then_inc(c_ev, 1)

            def u_evac(v, c, e):
                act.wait_ge(u_mm, v + 3)
                act.wait_ge(u_done, v + 1)
                fn(up[:, e, TAPS - 1:TAPS - 1 + T], ps_u[:, 0:T], ACT.Copy)
                fn(cv[:, e, :], ps_u[:, 0:T], ACT.Identity, bias=cb[:, bass.ds(c, 1)],
                   scale=cw[:, bass.ds(c, 1), TAPS - 1]).then_inc(u_ev, 1)

            def u_tanh(v, e):
                act.wait_ge(conv_step, 3 * v + 3)
                fn(th[:, e, :], cv[:, e, :], ACT.Tanh).then_inc(th_done, 1)

            def norm(j):
                act.wait_ge(wx_mm, NC * (j + 1) + 2)
                fn(xs[:, :], ps_x[0:RX, 0:T], ACT.Copy).then_inc(act_step, 1)
                fn(sq[:, :], ps_x[0:RX, 0:T], ACT.Square).then_inc(act_step, 1)
                act.wait_ge(act_step, 2 * j + 2)
                act.sem_inc(x_ev, 1)
                act.wait_ge(ms_mm, j + 1)
                fn(rr[:, :], S[0:RX, 0:T], ACT.Ln, bias=eps[:, :]).then_inc(ms_ev, 1)
                act.wait_ge(ms_ev, j + 1)
                fn(rr[:, :], rr[:, :], ACT.Exp, scale=-0.5).then_inc(r_done, 1)

            def softplus(j):
                for c in range(NC):
                    act.wait_ge(z_mm, NC * j + c + 1)
                    fn(dy[:, c, :], Yring[c % 2][:, 0:T], ACT.Identity, bias=dtb[:, c:c + 1]).then_inc(z_ev, 1)
                act.wait_ge(z_ev, NC * (j + 1))
                zt = dy[:, :, :].rearrange("p c t -> p (c t)")
                tmp = st[:, :, :, :].rearrange("p q n t -> p (q n t)")
                fn(tmp, zt, ACT.Abs).then_inc(sp_step, 1)
                act.wait_ge(sp_step, 3 * j + 1)
                fn(tmp, tmp, ACT.Exp, scale=-1.0).then_inc(sp_step, 1)
                act.wait_ge(sp_step, 3 * j + 2)
                fn(tmp, tmp, ACT.Ln, bias=1.0).then_inc(sp_step, 1)

            def spread_out(j):
                act.wait_ge(nrm_done, j + 1)
                act.dma_start(bc_rows[bass.ds(j, 1)].rearrange("a n t -> (a n) t"), nrm[R:RX, :]).then_inc(bc_st, 16)

            def spread_in(j):
                if not (isinstance(j, int) and j == 0):
                    act.wait_ge(hc_done, Q * NC * j)
                act.wait_ge(bc_st, 16 * (j + 1))
                act.dma_start(bc[:, :, :, :].rearrange("p a n t -> p (a n t)"),
                              bc_rows[bass.ds(j, 1)].rearrange("a n t -> a (n t)").to_broadcast([P, 2 * N * T])
                              ).then_inc(bc_ld, 16)

            act.wait_ge(set_up, 1)
            act.wait_ge(consts_ld, 16 * N_CONSTS)
            act.wait_ge(halved, 2)
            act.wait_ge(gs_mm, 1)
            fn(g_gate[:, :, :].rearrange("p k e -> p (k e)"), S[:, 0:KH * E], ACT.Copy)
            fn(g_bias[:, :], S[:, 64:64 + EK], ACT.Copy)
            fn(gate_bias[:, :], S[0:1, 72:72 + E], ACT.Copy)
            fn(b2g_stage[:, E * ER:E * ER + E], S[:, 80:80 + E], ACT.Copy)
            fn(b2g_stage[:, 0:E * ER], Yring[0][:, :], ACT.Copy).then_inc(gs_ev, 1)
            cond(0, 0, KH)
            cond(1, 1, 2 * KH)
            with act.Fori(0, PAIRS) as p:
                for e in range(2):
                    u_evac(2 * p + e, 2 * p + e, e)
                    u_tanh(2 * p + e, e)
            norm(0)
            spread_out(0)
            for i in range(2):
                act.wait_ge(G_st[i], 16 * KH // 2)
            act.wait_ge(b2g_st, 16)
            softplus(0)
            spread_in(0)

            def slots(g, p, first):
                for e in range(2):
                    c = 2 * p + e
                    s = NC * g + c
                    for q in range(Q):
                        act.wait_ge(scan_done, Q * s + q + 1)
                        if q == 0:
                            act.wait_ge(delta_done, g + 1)
                        for n in range(NQ):
                            last = fn(dA[:, q, n, 1:T], dy[:, bass.ds(c, 1), 1:T].rearrange("p a t -> p (a t)"),
                                      ACT.Exp, scale=A_sb[:, bass.ds(c * N + (q * NQ + n), 1)])
                        last.then_inc(dA_done, 1)
                        if q == 1 and has_next(g) and not (first and e == 0):
                            u_tanh(s + NC - 1, 1 - e)
                    act.wait_ge(gate_mm, s + 3)
                    act.wait_ge(y_done, s + 1)
                    fn(gh[:, e, :], ps_gate[:, 0:T], ACT.Copy, scale=0.5)
                    fn(gt[:, e, :], ps_gate[:, 0:T], ACT.Tanh, scale=0.5).then_inc(gate_ev, 1)
                    if has_next(g):
                        u_evac(s + NC, c, e)

            def group(g):
                tb = tiles_before(g)
                slots(g, 0, True)
                with act.Fori(1, PAIRS) as p:
                    slots(g, p, False)
                if has_next(g):
                    u_tanh(NC * (g + 2) - 1, 1)
                    norm(g + 1)
                    spread_out(g + 1)
                    softplus(g + 1)
                    spread_in(g + 1)
                act.wait_ge(la2_mm, g + 1)
                fn(la2[:, :], S[0:LR, 0:T], ACT.Copy).then_inc(la2_ev, 1)
                act.wait_ge(lg_mm, g + 1)
                fn(lg[:, :, :].rearrange("p a e -> p (a e)"), S[:, 0:2 * E], ACT.Copy).then_inc(lg_ev, 1)
                for m in range(EK):
                    act.wait_ge(m_mm, RING + tb + OUT_TILES + m + 1)
                    fn(hw[:, m, :], Yring[m % 2][:, 0:T], ACT.Identity, bias=g_bias[:, m:m + 1]).then_inc(h_ev, 1)
                act.wait_ge(soft, SOFT_STEPS * g + 2)
                fn(ex[:, :, :], lm[:, :, :], ACT.Exp).then_inc(ex_done, 1)
                if has_cond(g):
                    cond(g + 2, g % 2, tb + OUT_TILES + G_TILES)
                act.wait_ge(wT_mm, g + 1)
                fn(wT[:, :], S[0:E, 0:T], ACT.Copy).then_inc(wT_ev, 1)
                for h in range(2):
                    act.wait_ge(d_ev, 2 + PRO_D + D_USES * g + KH + EK + (h + 1) * KH // 2)
                    act.dma_start(out[bass.ds(g, 1)].rearrange("a p k t -> p (a k) t")[:, h * KH // 2:(h + 1) * KH // 2, :],
                                  x2[:, h * KH // 2:(h + 1) * KH // 2, :]).then_inc(out_st, 16)

            with act.Fori(0, B - 2) as g:
                group(g)
            group(B - 2)
            group(B - 1)

        @block.vector
        def _(dve):
            v_ = nc.vector
            dve.sem_inc(gate_mm, 2)
            dve.sem_inc(u_mm, 2)
            dve.sem_inc(wx_mm, 2)
            dve.sem_inc(u_done, 2)
            dve.sem_inc(scan_done, Q)
            dve.sem_inc(y_mm, Q)
            dve.sem_inc(y_done, 2)
            dve.sem_inc(m_mm, RING)
            dve.sem_inc(d_ev, 2)
            dve.sem_inc(gate_ev, 1)
            dve.sem_inc(h_ev, 1)
            dve.sem_inc(wT_ev, 1)
            dve.sem_inc(out_st, 16)
            v_.memset(ones_row[:, :], 1.0)
            v_.memset(eps[:, :], 1e-6)
            v_.memset(dA[:, :, :, :], 0.0)
            v_.memset(up[:, :, :], 0.0).then_inc(set_up, 1)
            dve.wait_ge(consts_ld, 16 * N_CONSTS)
            v_.tensor_scalar(cw[:, :, :], cw[:, :, :], 0.5, None, ALU.mult).then_inc(halved, 1)
            v_.tensor_scalar(cb[:, :], cb[:, :], 0.5, None, ALU.mult).then_inc(halved, 1)
            for m in range(KH):
                dve.wait_ge(G_mm, m + 1)
                if m >= 2:
                    dve.wait_ge(G_st[m % 2], 16 * (m // 2))
                v_.tensor_copy(stage[m % 2], Dring[m % 2][:, :]).then_inc(G_ev, 1)
                dve.sem_inc(d_ev, 1)

            def conv(v, c, e):
                dve.wait_ge(u_ev, v + 1)
                for i in range(TAPS - 1):
                    if i:
                        dve.wait_ge(conv_step, 3 * v + i)
                    v_.scalar_tensor_tensor(cv[:, e, :], up[:, e, i:i + T], cw[:, bass.ds(c, 1), i], cv[:, e, :],
                                            ALU.mult, ALU.add).then_inc(conv_step, 1)

            def u_out(v, c, e):
                dve.wait_ge(th_done, v + 1)
                v_.scalar_tensor_tensor(u_sb[:, bass.ds(c, 1), :].rearrange("p a t -> p (a t)"), th[:, e, :], 1.0,
                                        cv[:, e, :], ALU.add, ALU.mult).then_inc(u_done, 1)

            def norm(j):
                dve.wait_ge(r_done, j + 1)
                v_.scalar_tensor_tensor(nrm[:, :], xs[:, :], lnw[:, 0:1], rr[:, :], ALU.mult, ALU.mult
                                        ).then_inc(nrm_done, 1)

            def delta(j):
                dve.wait_ge(sp_step, 3 * j + 3)
                zt = dy[:, :, :].rearrange("p c t -> p (c t)")
                v_.scalar_tensor_tensor(zt, zt, 0.0, st[:, :, :, :].rearrange("p q n t -> p (q n t)"),
                                        ALU.max, ALU.add).then_inc(delta_done, 1)

            dve.wait_ge(halved, 2)
            with dve.Fori(0, PAIRS) as p:
                for e in range(2):
                    conv(2 * p + e, 2 * p + e, e)
                    u_out(2 * p + e, 2 * p + e, e)
            norm(0)
            delta(0)

            def y_out(s, c, e):
                dve.wait_ge(gate_ev, s + 2)
                v_.scalar_tensor_tensor(gh[:, e, :], gt[:, e, :], 1.0, gh[:, e, :], ALU.add, ALU.mult
                                        ).then_inc(y_step, 1)
                dve.wait_ge(y_mm, Q + Q * (s + 1))
                v_.scalar_tensor_tensor(y1[:, :], u_sb[:, bass.ds(c, 1), :].rearrange("p a t -> p (a t)"),
                                        D_sb[:, bass.ds(c, 1)], Yring[e][:, 0:T], ALU.mult, ALU.add
                                        ).then_inc(y_step, 1)
                dve.wait_ge(y_step, 2 * s + 2)
                v_.tensor_tensor(dy[:, bass.ds(c, 1), :].rearrange("p a t -> p (a t)"), gh[:, e, :], y1[:, :],
                                 ALU.mult).then_inc(y_done, 1)

            def slots(g, p, first):
                for e in range(2):
                    c = 2 * p + e
                    s = NC * g + c
                    for q in range(Q):
                        dve.wait_ge(dA_done, Q * s + q + 1)
                        dve.wait_ge(dbu_done, Q * s + q + 1)
                        stq = st[:, q, :, :].rearrange("p n t -> p (n t)")
                        v_.tensor_tensor_scan(stq, dA[:, q, :, :].rearrange("p n t -> p (n t)"), stq, 0.0,
                                              ALU.mult, ALU.add).then_inc(scan_done, 1)
                        dve.wait_ge(scan_done, Q + Q * s + q + 1)
                        v_.tensor_tensor(stq, stq, bc[:, 1, q * NQ:(q + 1) * NQ, :].rearrange("p n t -> p (n t)"),
                                         ALU.mult).then_inc(hc_done, 1)
                        late = not (first and e == 0)
                        if q == 0 and late:
                            y_out(s - 1, c - 1, 1 - e)
                        if q == 1 and late and has_next(g):
                            u_out(s + NC - 1, c - 1, 1 - e)
                        if q == 3 and has_next(g):
                            conv(s + NC, c, e)

            def group(g):
                tb = tiles_before(g)
                dve.wait_ge(bc_ld, 16 * (g + 1))
                slots(g, 0, True)
                with dve.Fori(1, PAIRS) as p:
                    slots(g, p, False)
                y_out(NC * (g + 1) - 1, NC - 1, 1)
                if has_next(g):
                    u_out(NC * (g + 2) - 1, NC - 1, 1)
                dve.wait_ge(ffn_ld, 48 * g + 48)
                for m in range(KH):
                    dve.wait_ge(m_mm, RING + tb + 2 * m + 2)
                    v_.tensor_tensor(x2[:, m, :], x2[:, m, :], Dring[m % 2][:, 0:T], ALU.add).then_inc(d_ev, 1)
                if has_next(g):
                    norm(g + 1)
                    delta(g + 1)
                s0 = SOFT_STEPS * g
                mx, z, rz, s2, rs = (sc[:, i, :] for i in range(5))
                dve.wait_ge(lg_ev, g + 1)
                v_.tensor_reduce(mx, lg[:, :, :], AX.X, ALU.max).then_inc(soft, 1)
                dve.wait_ge(soft, s0 + 1)
                v_.tensor_scalar(lm[:, 0, :], lg[:, 0, :], mx[:, 0:1], None, ALU.subtract)
                v_.tensor_scalar(lm[:, 1, :], lg[:, 1, :], mx[:, 1:2], None, ALU.subtract).then_inc(soft, 1)
                dve.wait_ge(ex_done, g + 1)
                v_.tensor_reduce(z, ex[:, :, :], AX.X, ALU.add).then_inc(soft, 1)
                dve.wait_ge(soft, s0 + 3)
                v_.reciprocal(rz, z).then_inc(soft, 1)
                dve.wait_ge(soft, s0 + 4)
                for t in range(2):
                    last = v_.tensor_scalar(pr[:, t, :], ex[:, t, :], rz[:, t:t + 1], None, ALU.mult)
                last.then_inc(soft, 1)
                dve.wait_ge(soft, s0 + 5)
                v_.tensor_copy(pr_copy[:, :, :], pr[:, :, :])
                for t in range(2):
                    last = v_.max(top[:, t, :], pr[:, t, :])
                last.then_inc(soft, 1)
                dve.wait_ge(soft, s0 + 6)
                v_.tensor_tensor(s2, top[:, :, 0], top[:, :, 1], ALU.add).then_inc(soft, 1)
                for t in range(2):
                    last = v_.max_index(tix[:, t, :], top[:, t, :], pr[:, t, :])
                last.then_inc(soft, 1)
                dve.wait_ge(soft, s0 + 8)
                v_.tensor_copy(tixf[:, :, :], tix[:, :, :]).then_inc(soft, 1)
                v_.reciprocal(rs, s2).then_inc(soft, 1)
                dve.wait_ge(soft, s0 + 10)
                for t in range(2):
                    last = v_.tensor_scalar(w01[:, t, :], top[:, t, 0:2], rs[:, t:t + 1], None, ALU.mult)
                last.then_inc(soft, 1)
                dve.wait_ge(soft, s0 + 11)
                for t in range(2):
                    for i in range(2):
                        v_.tensor_scalar(oh[:, i, t, :], iota[:, :], tixf[:, t, i:i + 1], w01[:, t, i:i + 1],
                                         ALU.is_equal, ALU.mult).then_inc(soft, 1)
                dve.wait_ge(soft, s0 + 15)
                v_.tensor_tensor(wf[:, :, :], oh[:, 0, :, :], oh[:, 1, :, :], ALU.add).then_inc(wf_done, 1)
                dve.sem_inc(soft, 1)
                dve.wait_ge(h_ev, EK * (g + 1) + 1)
                for m in range(EK):
                    dve.wait_ge(wb_mm, EK * g + m + 1)
                    v_.tensor_tensor(hw[:, m, :], hw[:, m, :], Dring[m % 2][:, 0:T], ALU.mult).then_inc(d_ev, 1)
                t0 = OUT_TILES + G_TILES + (COND_TILES if has_cond(g) else 0)
                for m in range(KH):
                    dve.wait_ge(m_mm, RING + tb + t0 + m // 2 + 1)
                    v_.tensor_tensor(x2[:, m, :], x2[:, m, :], Dring[m % 2][:, 0:T], ALU.add).then_inc(d_ev, 1)

            with dve.Fori(0, B - 2) as g:
                group(g)
            group(B - 2)
            group(B - 1)

        @block.gpsimd
        def _(pool):
            for m in range(KH):
                pool.wait_ge(G_ev, m + 1)
                pool.dma_start(G_tiles[:, :, m, :].rearrange("g p c -> p g c"),
                               stage[m % 2].rearrange("p (g c) -> p g c", g=EK)).then_inc(G_st[m % 2], 16)
            pool.wait_ge(gs_ev, 1)
            pool.dma_start(b2g_rows.rearrange("b r c -> (b r) c"), b2g_stage).then_inc(b2g_st, 16)

            def group(g):
                with pool.Fori(0, PAIRS) as p:
                    for e in range(2):
                        c = 2 * p + e
                        s = NC * g + c
                        if e == 0:
                            pool.wait_ge(delta_done, g + 1)
                            pool.wait_ge(u_done, NC * (g + 1) + 2)
                            pool.wait_ge(bc_ld, 16 * (g + 1))
                        nc.gpsimd.tensor_tensor(w_sb[:, e, :], dy[:, bass.ds(c, 1), :].rearrange("p a t -> p (a t)"),
                                                u_sb[:, bass.ds(c, 1), :].rearrange("p a t -> p (a t)"),
                                                ALU.mult).then_inc(w_done, 1)
                        pool.wait_ge(w_done, s + 1)
                        for q in range(Q):
                            pool.wait_ge(y_mm, Q * s + q + 1)
                            nc.gpsimd.tensor_tensor(st[:, q, :, :], w_sb[:, e:e + 1, :].to_broadcast([P, NQ, T]),
                                                    bc[:, 0, q * NQ:(q + 1) * NQ, :], ALU.mult).then_inc(dbu_done, 1)

            with pool.Fori(0, B - 2) as g:
                group(g)
            group(B - 2)
            group(B - 1)
            pool.wait_ge(out_st, 32 * B + 16)
            pool.wait_ge(bc_st, 16 * B)
            for i in range(2):
                pool.wait_ge(G_st[i], 16 * KH // 2)
            pool.wait_ge(b2g_st, 16)


def kernel(**inputs):
    import concourse.bacc as bacc
    from concourse.bass_utils import run_bass_kernel_spmd

    a = {k: np.asarray(v) for k, v in inputs.items()}

    def cols(v):
        return v.reshape(-1, P).T

    def tiles(w):
        o, i = w.shape
        return w.reshape(o // P, P, i // P, P).transpose(0, 3, 2, 1)

    mean = np.zeros((RX, RX), np.float32)
    for lo, hi in ((0, R), (R, R + N), (R + N, RX)):
        mean[lo:hi, lo:hi] = 1.0 / (hi - lo)
    sel = np.repeat(np.eye(E, dtype=np.float32), ER, axis=1)
    experts = a["L0_ffn_lora_A"].reshape(E * ER, KH, P).transpose(2, 1, 0)
    ffn_b = a["L0_ffn_lora_B"].reshape(E, LB_TILES, 2, P, ER)
    ffn_b = ffn_b.reshape(EK, 2, LB_TILES, 2, P, ER).transpose(2, 1, 5, 3, 0, 4)
    lay = [
        ("x", a["x"].reshape(B, T, KH, P).transpose(0, 3, 2, 1)),
        ("idx_cond", a["itok_B_0_23"].reshape(1, B)),
        ("idx_cond2", a["itok_B_6_15"].reshape(1, B)),
        ("cond_W", tiles(a["L0_cond_W"])),
        ("cond_b", cols(a["L0_cond_b"])),
        ("cond_A", a["L0_cond_lora_As"].reshape(SLOTS, KH, P, LR).transpose(0, 2, 1, 3)),
        ("cond_B", a["L0_cond_lora_Bs"]),
        ("W_in", tiles(a["L0_attn_W_in"])),
        ("conv_w", a["L0_attn_conv_w"].reshape(NC, P, TAPS).transpose(1, 0, 2)),
        ("conv_b", cols(a["L0_attn_conv_b"])),
        ("Wx", a["L0_attn_Wx"].reshape(RX, NC, P).transpose(1, 2, 0)),
        ("ln_dt", a["L0_attn_dt_ln_w"].reshape(R, 1)),
        ("ln_b", a["L0_attn_b_ln_w"].reshape(N, 1)),
        ("ln_c", a["L0_attn_c_ln_w"].reshape(N, 1)),
        ("Wdt", a["L0_attn_Wdt"].T),
        ("dt_bias", cols(a["L0_attn_dt_bias"])),
        ("A_mat", a["L0_attn_A"].reshape(NC, P, N).transpose(1, 0, 2).reshape(P, NC * N)),
        ("D_par", cols(a["L0_attn_D_param"])),
        ("W_out", tiles(a["L0_attn_W_out"]).reshape(KH, P, 2, KH, P).transpose(0, 2, 1, 3, 4)),
        ("base_W", tiles(a["L0_cond2_base_weight"].T)),
        ("base_b", cols(a["L0_cond2_base_bias"])),
        ("lora2_A", a["L0_cond2_lora_A_w"].reshape(SLOTS, LR, KH, P).transpose(0, 3, 2, 1)),
        ("lora2_B", a["L0_cond2_lora_B_w"].reshape(SLOTS, KH, P, LR).transpose(0, 2, 1, 3)),
        ("GT_gate", a["L0_ffn_gate_w"].reshape(E, KH, P).transpose(2, 1, 0)),
        ("GT_exp", experts),
        ("ffn_B", ffn_b.reshape(LB_TILES, P, 2 * EK, P)),
        ("ident", np.eye(P, dtype=np.float32)),
        ("mean", mean),
        ("sel", sel),
        ("iota", np.tile(np.arange(E, dtype=np.float32), (P, 1))),
    ]
    nc = bacc.Bacc("TRN2", target_bir_lowering=False, num_devices=1)
    arrays, aps = {}, {}
    for name, v in lay:
        v = np.ascontiguousarray(v)
        arrays["in_" + name] = v
        aps[name] = nc.dram_tensor("in_" + name, v.shape, mybir.dt.from_np(v.dtype), kind="ExternalInput").ap()
    out = nc.dram_tensor("out", (B, P, KH, T), F32, kind="ExternalOutput").ap()
    ln = [aps.pop("ln_dt"), aps.pop("ln_b"), aps.pop("ln_c")]
    args = [aps[n] for n, _ in lay if n in aps]
    at = [n for n, _ in lay if n in aps].index("Wdt")
    build(nc, *args[:at], ln, *args[at:], out)
    r = run_bass_kernel_spmd(nc, [arrays], core_ids=[0])
    got = r.results[0]["out"]
    return got.transpose(0, 3, 2, 1).reshape(B, T, H)
```
